# Optimizing a Trainium2 kernel written in Bass

```python
import numpy as np
import jax
import jax.numpy as jnp

def _softmax(x, axis=-1):
    return jax.nn.softmax(x, axis=axis)

def _gelu(x):
    return jax.nn.gelu(x, approximate=True)

def _silu(x):
    return jax.nn.silu(x)

def _sigmoid(x):
    return jax.nn.sigmoid(x)

def _layernorm(x, axis=-1, eps=1e-05):
    m = jnp.mean(x, axis=axis, keepdims=True)
    v = jnp.var(x, axis=axis, keepdims=True)
    return (x - m) / jnp.sqrt(v + eps)

def _scatter_add(tgt, idx, src, axis=0):
    return tgt.at[idx].add(src)

def _segment_sum(src, seg, n):
    return jax.ops.segment_sum(src, seg, n)
kernel_name = 'mk_hybrid_d1_jaxref_r8_97252c'

def setup_inputs(seed: int=0):
    np.random.seed(seed)
    _w = jnp.asarray

    def _L0_attn_a_setup():
        import math
        import jax, jax.numpy as jnp
        import numpy as np
        N_HEAD = 16
        X_INT = -100.0
        Y_INT = 1.0
        POWER = 2
        DIVISOR = 1000.0

        def polymax(x):
            m = Y_INT / X_INT
            lin_cond = (x >= X_INT) & (x <= 0)
            x_lin = jnp.where(lin_cond, x, 0.0)
            lin = jnp.where(lin_cond, m * x_lin + Y_INT, 0.0)
            pos_cond = x > 0
            x_pos = jnp.where(pos_cond, x, 0.0)
            poly = jnp.where(pos_cond, x_pos ** POWER + Y_INT, 0.0)
            return (poly + lin) / DIVISOR
        key = jax.random.key(seed)
        k1, k2, k3 = jax.random.split(key, 3)
        B, T, C = (2, 256, 128)
        x = jax.random.normal(k1, (B, T, C), dtype=jnp.float32)
        W_attn = jax.random.normal(k2, (C, 3 * C), dtype=jnp.float32) * (1.0 / math.sqrt(C))
        W_proj = jax.random.normal(k3, (C, C), dtype=jnp.float32) * (1.0 / math.sqrt(C))
        return {'x': x, 'W_attn': W_attn, 'W_proj': W_proj}
    _L0_attn_a_in = _L0_attn_a_setup()

    def _L0_attn_b_setup():
        import jax, jax.numpy as jnp
        import numpy as np
        D_MODEL = 128
        NUM_HEADS = 16
        DK = D_MODEL // NUM_HEADS
        key = jax.random.key(seed)
        kx, kq, kk, kv, ko = jax.random.split(key, 5)
        B, S = (4, 256)
        bound = float(np.sqrt(6.0 / (D_MODEL + D_MODEL)))
        uni = lambda k: jax.random.uniform(k, (D_MODEL, D_MODEL), jnp.float32, -bound, bound)
        return {'x': jax.random.normal(kx, (B, S, D_MODEL), jnp.float32), 'q_heads': uni(kq), 'k_heads': uni(kk), 'v_heads': uni(kv), 'output_proj': uni(ko)}
    _L0_attn_b_in = _L0_attn_b_setup()

    def _L0_ffn_setup():
        import jax, jax.numpy as jnp
        import numpy as np
        DIM = 128
        DEPTH = 6
        HEADS = 16
        DIM_HEAD = 64
        WINDOW = 32
        INNER = HEADS * DIM_HEAD
        DIM_INNER = int(DIM * 4 * 2 / 3)
        QK_SCALE = 8.0

        def shift_tokens(t):
            a, s = jnp.split(t, 2, -1)
            s = jnp.pad(s, ((0, 0), (1, 0), (0, 0)))[:, :-1]
            return jnp.concatenate([a, s], -1)

        def l2norm(t):
            return t / jnp.maximum(jnp.linalg.norm(t, axis=-1, keepdims=True), 1e-12)

        def rotate_half(x):
            x1, x2 = jnp.split(x, 2, -1)
            return jnp.concatenate([-x2, x1], -1)

        def rotary_tables(n):
            half = jnp.arange(0, DIM_HEAD, 2, dtype=jnp.float32)
            inv_freq = 1.0 / 10000.0 ** (half / DIM_HEAD)
            t = jnp.arange(n, dtype=jnp.float32)
            freqs = t[:, None] * inv_freq[None, :]
            freqs = jnp.concatenate([freqs, freqs], -1)
            base_scale = (half + 0.4 * DIM_HEAD) / (1.4 * DIM_HEAD)
            power = (t - n // 2) / (WINDOW // 2)
            scale = base_scale[None, :] ** power[:, None]
            scale = jnp.concatenate([scale, scale], -1)
            return (freqs, scale)

        def local_attention(q, k, v):
            b, h, n, d = q.shape
            w = WINDOW
            nw = n // w
            bq = q.reshape(b, h, nw, w, d)
            bk = k.reshape(b, h, nw, w, d)
            bv = v.reshape(b, h, nw, w, d)

            def look(t):
                p = jnp.pad(t, ((0, 0), (0, 0), (1, 0), (0, 0), (0, 0)))
                return jnp.concatenate([p[:, :, :nw], p[:, :, 1:]], axis=3)
            bk2, bv2 = (look(bk), look(bv))
            seq = jnp.arange(n).reshape(nw, w)
            seq_p = jnp.pad(seq, ((1, 0), (0, 0)), constant_values=-1)
            jt = jnp.concatenate([seq_p[:nw], seq_p[1:]], axis=1)
            it = seq[:, :, None]
            jb = jt[:, None, :]
            mask = (it < jb) | (it > jb + w) | (jb == -1)
            sim = jnp.einsum('bhwie,bhwje->bhwij', bq, bk2) * QK_SCALE
            sim = jnp.where(mask, -jnp.finfo(sim.dtype).max, sim)
            attn = jax.nn.softmax(sim, -1)
            out = jnp.einsum('bhwij,bhwje->bhwie', attn, bv2)
            return out.reshape(b, h, n, d)

        def attn_layer(x, Wqkv, qs, ksc, Wo):
            b, n, _ = x.shape
            qkv = x @ Wqkv
            q, k, v = jnp.split(qkv, 3, -1)
            sh = lambda t: t.reshape(b, n, HEADS, DIM_HEAD).transpose(0, 2, 1, 3)
            q, k, v = (sh(q), sh(k), sh(v))
            q = l2norm(q) * qs
            k = l2norm(k) * ksc
            freqs, scale = rotary_tables(n)
            cos, sin = (jnp.cos(freqs), jnp.sin(freqs))
            q = q * cos * scale + rotate_half(q) * sin * scale
            inv = 1.0 / scale
            k = k * cos * inv + rotate_half(k) * sin * inv
            out = local_attention(q, k, v)
            out = out.transpose(0, 2, 1, 3).reshape(b, n, INNER)
            return out @ Wo

        def ffn_layer(x, g, bln, W1, b1, W2, b2):
            mu = x.mean(-1, keepdims=True)
            var = ((x - mu) ** 2).mean(-1, keepdims=True)
            xn = (x - mu) / jnp.sqrt(var + 1e-05) * g + bln
            hg = xn @ W1 + b1
            a, gate = jnp.split(hg, 2, -1)
            return a * jax.nn.gelu(gate, approximate=False) @ W2 + b2
        key = jax.random.key(seed)
        ks = jax.random.split(key, 8)
        B, N = (2, 256)
        init = lambda k, shape: jax.random.normal(k, shape, jnp.float32) * 0.02
        return {'x': jax.random.normal(ks[0], (B, N, DIM), jnp.float32), 'Wqkv': init(ks[1], (DEPTH, DIM, 3 * INNER)), 'q_scale': jnp.ones((DEPTH, DIM_HEAD), jnp.float32), 'k_scale': jnp.ones((DEPTH, DIM_HEAD), jnp.float32), 'Wo': init(ks[2], (DEPTH, INNER, DIM)), 'ln_g': jnp.ones((DEPTH, DIM), jnp.float32), 'ln_b': jnp.zeros((DEPTH, DIM), jnp.float32), 'W1': init(ks[3], (DEPTH, DIM, 2 * DIM_INNER)), 'b1': jnp.zeros((DEPTH, 2 * DIM_INNER), jnp.float32), 'W2': init(ks[4], (DEPTH, DIM_INNER, DIM)), 'b2': jnp.zeros((DEPTH, DIM), jnp.float32)}
    _L0_ffn_in = _L0_ffn_setup()
    _d = {'L0_attn_a_x': _L0_attn_a_in['x'], 'L0_attn_a_W_attn': _L0_attn_a_in['W_attn'], 'L0_attn_a_W_proj': _L0_attn_a_in['W_proj'], 'L0_attn_b_q_heads': _L0_attn_b_in['q_heads'], 'L0_attn_b_k_heads': _L0_attn_b_in['k_heads'], 'L0_attn_b_v_heads': _L0_attn_b_in['v_heads'], 'L0_attn_b_output_proj': _L0_attn_b_in['output_proj'], 'L0_ffn_Wqkv': _L0_ffn_in['Wqkv'], 'L0_ffn_q_scale': _L0_ffn_in['q_scale'], 'L0_ffn_k_scale': _L0_ffn_in['k_scale'], 'L0_ffn_Wo': _L0_ffn_in['Wo'], 'L0_ffn_ln_g': _L0_ffn_in['ln_g'], 'L0_ffn_ln_b': _L0_ffn_in['ln_b'], 'L0_ffn_W1': _L0_ffn_in['W1'], 'L0_ffn_b1': _L0_ffn_in['b1'], 'L0_ffn_W2': _L0_ffn_in['W2'], 'L0_ffn_b2': _L0_ffn_in['b2']}
    _x0 = _d['L0_attn_a_x']
    _d['L0_attn_a_x'] = jax.random.normal(jax.random.fold_in(jax.random.key(seed), 1), (2, 1024, 128), dtype=_x0.dtype)
    del _x0
    return _d

def reference(L0_attn_a_x, L0_attn_a_W_attn, L0_attn_a_W_proj, L0_attn_b_q_heads, L0_attn_b_k_heads, L0_attn_b_v_heads, L0_attn_b_output_proj, L0_ffn_Wqkv, L0_ffn_q_scale, L0_ffn_k_scale, L0_ffn_Wo, L0_ffn_ln_g, L0_ffn_ln_b, L0_ffn_W1, L0_ffn_b1, L0_ffn_W2, L0_ffn_b2):

    def _L0_attn_a_ref(x, W_attn, W_proj):
        import math
        import jax, jax.numpy as jnp
        import numpy as np
        N_HEAD = 16
        X_INT = -100.0
        Y_INT = 1.0
        POWER = 2
        DIVISOR = 1000.0

        def polymax(x):
            m = Y_INT / X_INT
            lin_cond = (x >= X_INT) & (x <= 0)
            x_lin = jnp.where(lin_cond, x, 0.0)
            lin = jnp.where(lin_cond, m * x_lin + Y_INT, 0.0)
            pos_cond = x > 0
            x_pos = jnp.where(pos_cond, x, 0.0)
            poly = jnp.where(pos_cond, x_pos ** POWER + Y_INT, 0.0)
            return (poly + lin) / DIVISOR
        B, T, C = x.shape
        H = N_HEAD
        hd = C // H
        qkv = x @ W_attn
        q, k, v = jnp.split(qkv, 3, axis=-1)
        q = q.reshape(B, T, H, hd).transpose(0, 2, 1, 3)
        k = k.reshape(B, T, H, hd).transpose(0, 2, 1, 3)
        v = v.reshape(B, T, H, hd).transpose(0, 2, 1, 3)
        att = jnp.einsum('bhid,bhjd->bhij', q, k) * (1.0 / math.sqrt(hd))
        causal = jnp.tril(jnp.ones((T, T), dtype=bool))
        att = jnp.where(causal[None, None], att, -jnp.inf)
        att = polymax(att)
        y = jnp.einsum('bhij,bhjd->bhid', att, v)
        y = y.transpose(0, 2, 1, 3).reshape(B, T, C)
        return y @ W_proj

    def _L0_attn_b_ref(x, q_heads, k_heads, v_heads, output_proj):
        import jax, jax.numpy as jnp
        import numpy as np
        D_MODEL = 128
        NUM_HEADS = 16
        DK = D_MODEL // NUM_HEADS
        B, S, _ = x.shape

        def proj(W):
            return (x @ W.T).reshape(B, S, NUM_HEADS, DK).transpose(0, 2, 1, 3)
        q, k, v = (proj(q_heads), proj(k_heads), proj(v_heads))
        scale = 1.0 / jnp.sqrt(jnp.asarray(DK, x.dtype))
        scores = jnp.einsum('bhqd,bhkd->bhqk', q, k) * scale
        causal = jnp.triu(jnp.ones((S, S), bool), k=1)
        scores = jnp.where(causal, jnp.asarray(-jnp.inf, scores.dtype), scores)
        attn = jax.nn.softmax(scores, axis=-1)
        out = jnp.einsum('bhqk,bhkd->bhqd', attn, v)
        out = out.transpose(0, 2, 1, 3).reshape(B, S, D_MODEL)
        return out @ output_proj.T

    def _L0_ffn_ref(x, Wqkv, q_scale, k_scale, Wo, ln_g, ln_b, W1, b1, W2, b2):
        import jax, jax.numpy as jnp
        import numpy as np
        DIM = 128
        DEPTH = 6
        HEADS = 16
        DIM_HEAD = 64
        WINDOW = 32
        INNER = HEADS * DIM_HEAD
        DIM_INNER = int(DIM * 4 * 2 / 3)
        QK_SCALE = 8.0

        def shift_tokens(t):
            a, s = jnp.split(t, 2, -1)
            s = jnp.pad(s, ((0, 0), (1, 0), (0, 0)))[:, :-1]
            return jnp.concatenate([a, s], -1)

        def l2norm(t):
            return t / jnp.maximum(jnp.linalg.norm(t, axis=-1, keepdims=True), 1e-12)

        def rotate_half(x):
            x1, x2 = jnp.split(x, 2, -1)
            return jnp.concatenate([-x2, x1], -1)

        def rotary_tables(n):
            half = jnp.arange(0, DIM_HEAD, 2, dtype=jnp.float32)
            inv_freq = 1.0 / 10000.0 ** (half / DIM_HEAD)
            t = jnp.arange(n, dtype=jnp.float32)
            freqs = t[:, None] * inv_freq[None, :]
            freqs = jnp.concatenate([freqs, freqs], -1)
            base_scale = (half + 0.4 * DIM_HEAD) / (1.4 * DIM_HEAD)
            power = (t - n // 2) / (WINDOW // 2)
            scale = base_scale[None, :] ** power[:, None]
            scale = jnp.concatenate([scale, scale], -1)
            return (freqs, scale)

        def local_attention(q, k, v):
            b, h, n, d = q.shape
            w = WINDOW
            nw = n // w
            bq = q.reshape(b, h, nw, w, d)
            bk = k.reshape(b, h, nw, w, d)
            bv = v.reshape(b, h, nw, w, d)

            def look(t):
                p = jnp.pad(t, ((0, 0), (0, 0), (1, 0), (0, 0), (0, 0)))
                return jnp.concatenate([p[:, :, :nw], p[:, :, 1:]], axis=3)
            bk2, bv2 = (look(bk), look(bv))
            seq = jnp.arange(n).reshape(nw, w)
            seq_p = jnp.pad(seq, ((1, 0), (0, 0)), constant_values=-1)
            jt = jnp.concatenate([seq_p[:nw], seq_p[1:]], axis=1)
            it = seq[:, :, None]
            jb = jt[:, None, :]
            mask = (it < jb) | (it > jb + w) | (jb == -1)
            sim = jnp.einsum('bhwie,bhwje->bhwij', bq, bk2) * QK_SCALE
            sim = jnp.where(mask, -jnp.finfo(sim.dtype).max, sim)
            attn = jax.nn.softmax(sim, -1)
            out = jnp.einsum('bhwij,bhwje->bhwie', attn, bv2)
            return out.reshape(b, h, n, d)

        def attn_layer(x, Wqkv, qs, ksc, Wo):
            b, n, _ = x.shape
            qkv = x @ Wqkv
            q, k, v = jnp.split(qkv, 3, -1)
            sh = lambda t: t.reshape(b, n, HEADS, DIM_HEAD).transpose(0, 2, 1, 3)
            q, k, v = (sh(q), sh(k), sh(v))
            q = l2norm(q) * qs
            k = l2norm(k) * ksc
            freqs, scale = rotary_tables(n)
            cos, sin = (jnp.cos(freqs), jnp.sin(freqs))
            q = q * cos * scale + rotate_half(q) * sin * scale
            inv = 1.0 / scale
            k = k * cos * inv + rotate_half(k) * sin * inv
            out = local_attention(q, k, v)
            out = out.transpose(0, 2, 1, 3).reshape(b, n, INNER)
            return out @ Wo

        def ffn_layer(x, g, bln, W1, b1, W2, b2):
            mu = x.mean(-1, keepdims=True)
            var = ((x - mu) ** 2).mean(-1, keepdims=True)
            xn = (x - mu) / jnp.sqrt(var + 1e-05) * g + bln
            hg = xn @ W1 + b1
            a, gate = jnp.split(hg, 2, -1)
            return a * jax.nn.gelu(gate, approximate=False) @ W2 + b2
        for i in range(DEPTH):
            x = attn_layer(shift_tokens(x), Wqkv[i], q_scale[i], k_scale[i], Wo[i]) + x
            x = ffn_layer(shift_tokens(x), ln_g[i], ln_b[i], W1[i], b1[i], W2[i], b2[i]) + x
        return x
    x = L0_attn_a_x
    x = x + _L0_attn_a_ref(_layernorm(x, axis=-1), L0_attn_a_W_attn, L0_attn_a_W_proj)
    x = x + _L0_ffn_ref(_layernorm(x, axis=-1), L0_ffn_Wqkv, L0_ffn_q_scale, L0_ffn_k_scale, L0_ffn_Wo, L0_ffn_ln_g, L0_ffn_ln_b, L0_ffn_W1, L0_ffn_b1, L0_ffn_W2, L0_ffn_b2)
    x = x + _L0_attn_b_ref(_layernorm(x, axis=-1), L0_attn_b_q_heads, L0_attn_b_k_heads, L0_attn_b_v_heads, L0_attn_b_output_proj)
    x = x + _L0_ffn_ref(_layernorm(x, axis=-1), L0_ffn_Wqkv, L0_ffn_q_scale, L0_ffn_k_scale, L0_ffn_Wo, L0_ffn_ln_g, L0_ffn_ln_b, L0_ffn_W1, L0_ffn_b1, L0_ffn_W2, L0_ffn_b2)
    return x

_drawn_inputs = setup_inputs


def setup_inputs(seed=0):
    import zlib

    import numpy as np

    out = dict(_drawn_inputs(seed))
    spreads = {'L0_ffn_q_scale': (1.0, 0.6),
     'L0_ffn_k_scale': (1.0, 0.6),
     'L0_ffn_ln_g': (1.0, 0.6),
     'L0_ffn_ln_b': (0.0, 0.8),
     'L0_ffn_b1': (0.0, 0.575),
     'L0_ffn_b2': (0.0, 0.1)}
    factors = {}
    for name, (base, spread) in spreads.items():
        noise = np.random.default_rng([zlib.crc32(name.encode()), seed]).standard_normal(out[name].shape)
        drawn = base * np.exp(spread * noise) if base else spread * noise
        out[name] = jnp.asarray(drawn.astype(out[name].dtype))
    for name, factor in factors.items():
        out[name] = (out[name] * factor).astype(out[name].dtype)
    return out
```

```python
import math
from contextlib import ExitStack

import numpy as np

import concourse.bass as bass
from concourse import mybir

FP32 = mybir.dt.float32
BF16 = mybir.dt.bfloat16
I32 = mybir.dt.int32
ALU = mybir.AluOpType
ACT = mybir.ActivationFunctionType
AX = mybir.AxisListType

P = 128
B, T, C = 2, 1024, 128
N = B * T
TILES = N // P
TPB = T // P
HEADS = 16
HD = C // HEADS
DEPTH = 6
DH = 64
INNER = HEADS * DH
HP = INNER // P
W = 32
NG = P // W
DI = int(C * 4 * 2 / 3)
FCH = [(0, 128), (128, 128), (256, DI - 256)]
BLK = 512
NBLK = N // BLK
TB = BLK // P
SEQ = T + 1
EPS = 1e-5
NEG = -1e30
FFN_PARAMS = ["L0_ffn_Wqkv", "L0_ffn_q_scale", "L0_ffn_k_scale", "L0_ffn_Wo", "L0_ffn_ln_g", "L0_ffn_ln_b",
              "L0_ffn_W1", "L0_ffn_b1", "L0_ffn_W2", "L0_ffn_b2"]
RSQRT_SEED = float(0x5F3759DF)


class Sig:

    def __init__(self, sem, per=1, credit=0):
        self.sem, self.per, self.credit = sem, per, credit

    def at(self, n, j=None):
        return n * self.per + (self.credit * self.per + (self.per if j is None else j))

    def open(self, eng):
        eng.sem_inc(self.sem, self.credit * self.per)


def rsqrt_ops(nc, dve, ss, y, t, sig, n, floor):
    nc.vector.tensor_scalar(ss, ss, floor[0], floor[1], ALU.add, ALU.max).then_inc(sig.sem, 1)
    dve.wait_ge(sig.sem, sig.at(n, 1))
    nc.vector.tensor_scalar(t.bitcast(I32), ss.bitcast(I32), 1, None, ALU.logical_shift_right).then_inc(sig.sem, 1)
    dve.wait_ge(sig.sem, sig.at(n, 2))
    nc.vector.tensor_scalar(y.bitcast(I32), t.bitcast(I32), -1.0, RSQRT_SEED, ALU.mult, ALU.add).then_inc(sig.sem, 1)
    k = 3
    for _ in range(3):
        dve.wait_ge(sig.sem, sig.at(n, k))
        nc.vector.scalar_tensor_tensor(t, y, -0.5, y, ALU.mult, ALU.mult).then_inc(sig.sem, 1)
        dve.wait_ge(sig.sem, sig.at(n, k + 1))
        nc.vector.tensor_tensor(t, t, ss, ALU.mult).then_inc(sig.sem, 1)
        dve.wait_ge(sig.sem, sig.at(n, k + 2))
        nc.vector.scalar_tensor_tensor(y, t, 1.5, y, ALU.add, ALU.mult).then_inc(sig.sem, 1)
        k += 3


RSQRT_STEPS = 12


def combine_stats(nc, dve, bst, mean, var, dif, sig, n, k):
    nc.vector.tensor_tensor(mean[:], bst[:, :, 1], bst[:, :, 4], ALU.add).then_inc(sig.sem, 1)
    nc.vector.tensor_tensor(dif[:], bst[:, :, 1], bst[:, :, 4], ALU.subtract).then_inc(sig.sem, 1)
    nc.vector.tensor_tensor(var[:], bst[:, :, 2], bst[:, :, 5], ALU.add).then_inc(sig.sem, 1)
    dve.wait_ge(sig.sem, sig.at(n, k + 2))
    nc.vector.scalar_tensor_tensor(dif[:], dif[:], 0.25, dif[:], ALU.mult, ALU.mult).then_inc(sig.sem, 1)
    nc.vector.tensor_scalar(mean[:], mean[:], 0.5, None, ALU.mult).then_inc(sig.sem, 1)
    dve.wait_ge(sig.sem, sig.at(n, k + 5))
    nc.vector.scalar_tensor_tensor(var[:], var[:], 1.0 / C, dif[:], ALU.mult, ALU.add).then_inc(sig.sem, 1)
    dve.wait_ge(sig.sem, sig.at(n, k + 6))


def heads_of(ap, h=HEADS):
    return ap.rearrange("p (h d) -> p h d", h=h)


def over(ap, n):
    return ap.unsqueeze(2).to_broadcast([ap.shape[0], ap.shape[1], n])


def build_stack_kernel(nc, ins, outs):
    ctx = ExitStack()
    with ctx:
        def sb(name, shape, dt=FP32):
            return ctx.enter_context(nc.sbuf_tensor(name, shape, dt))

        PS = [ctx.enter_context(nc.psum_tensor(f"bank_pair{i}", [P, 1024], FP32)) for i in range(4)]
        X = sb("X", [P, N])
        H = sb("H", [P, B * SEQ])
        G = sb("G", [P, B * SEQ])
        ident = sb("ident", [P, P])
        ident16 = sb("ident16", [P, P], BF16)
        m = {"sems": ctx, "stack": {}, "X": X, "H": H, "G": G, "ident": ident, "ident16": ident16, "PS": PS}
        load_x(nc, ins, m)
        layer_norm(nc, m, "ln0")
        global_attention(nc, ins, m, "A")
        layer_norm(nc, m, "ln1")
        ffn_stack(nc, ins, m, 0)
        layer_norm(nc, m, "ln2")
        global_attention(nc, ins, m, "B")
        layer_norm(nc, m, "ln3")
        ffn_stack(nc, ins, m, 1)
        store_x(nc, outs, m)


def load_x(nc, ins, m):
    ctx = ExitStack()
    with ctx:
        xin = ctx.enter_context(nc.sbuf_tensor("xin", [P, TILES, C], FP32))
        x_in = m["sems"].enter_context(nc.semaphore("x_in"))
        ident_in = m["sems"].enter_context(nc.semaphore("ident_in"))
        x_tr = m["sems"].enter_context(nc.semaphore("x_transposed"))
        x_ev = m["sems"].enter_context(nc.semaphore("x_evacuated"))
        cleared = m["sems"].enter_context(nc.semaphore("states_cleared"))
        block = ctx.enter_context(nc.Block())

        @block.sync
        def _(sp):
            sp.dma_start(m["ident"][:], ins["ident"]).then_inc(ident_in, 16)
            sp.dma_start(m["ident16"][:], ins["ident16"].bitcast(BF16)).then_inc(ident_in, 16)
            for b in range(B):
                sp.dma_start(xin[:, b * TPB:(b + 1) * TPB, :],
                             ins["L0_attn_a_x"][b].rearrange("(t p) c -> p t c", p=P)).then_inc(x_in, 16)

        @block.vector
        def _(dve):
            nc.vector.memset(m["H"][:], 0.0).then_inc(cleared, 1)
            nc.vector.memset(m["G"][:], 0.0).then_inc(cleared, 1)

        @block.tensor
        def _(pe):
            pe.wait_ge(ident_in, 32)
            for b in range(B):
                pe.wait_ge(x_in, 32)
                for t in range(TPB):
                    nc.tensor.transpose(m["PS"][b][:, t * P:(t + 1) * P], xin[:, b * TPB + t, :],
                                        m["ident"][:]).then_inc(x_tr, 1)

        @block.scalar
        def _(act):
            for b in range(B):
                act.wait_ge(x_tr, (b + 1) * TPB)
                nc.scalar.activation(m["X"][:, b * T:(b + 1) * T], m["PS"][b][:], ACT.Copy).then_inc(x_ev, 1)


def store_x(nc, outs, m):
    ctx = ExitStack()
    with ctx:
        xout = ctx.enter_context(nc.sbuf_tensor("xout", [P, TILES, C], FP32))
        o_tr = m["sems"].enter_context(nc.semaphore("out_transposed"))
        o_ev = m["sems"].enter_context(nc.semaphore("out_evacuated"))
        o_out = m["sems"].enter_context(nc.semaphore("out_stored"))
        block = ctx.enter_context(nc.Block())

        @block.tensor
        def _(pe):
            for t in range(TILES):
                nc.tensor.transpose(m["PS"][t // TPB][:, (t % TPB) * P:(t % TPB + 1) * P],
                                    m["X"][:, t * P:(t + 1) * P], m["ident"][:]).then_inc(o_tr, 1)

        @block.scalar
        def _(act):
            for b in range(B):
                act.wait_ge(o_tr, (b + 1) * TPB)
                nc.scalar.activation(xout[:, b * TPB:(b + 1) * TPB, :].rearrange("p t c -> p (t c)"),
                                     m["PS"][b][:], ACT.Copy).then_inc(o_ev, 1)

        @block.sync
        def _(sp):
            for b in range(B):
                sp.wait_ge(o_ev, b + 1)
                sp.dma_start(outs["out"][b].rearrange("(t p) c -> p t c", p=P),
                             xout[:, b * TPB:(b + 1) * TPB, :]).then_inc(o_out, 16)
            sp.wait_ge(o_out, 32)


def layer_norm(nc, m, tag):
    ctx = ExitStack()
    with ctx:
        def sb(name, shape, dt=FP32):
            return ctx.enter_context(nc.sbuf_tensor(f"{tag}_{name}", shape, dt))

        def sem(name):
            return m["sems"].enter_context(nc.semaphore(f"{tag}_{name}"))

        bst = sb("bn_stats", [P, TILES, 6])
        mean, dif = sb("mean", [P, TILES]), sb("mean_gap", [P, TILES])
        var = sb("var", [P, TILES])
        rstd = sb("rstd", [P, TILES])
        tmp = sb("tmp", [P, TILES])
        xn = sb("xn", [P, TILES, C])
        PS = m["PS"]
        fwd, stats, newton = sem("to_tokens"), Sig(sem("stats"), TILES + 6), Sig(sem("rsqrt_steps"), RSQRT_STEPS)
        normed, back, evac = sem("normed"), sem("to_channels"), sem("evacuated")
        block = ctx.enter_context(nc.Block())

        @block.tensor
        def _(pe):
            for t in range(TILES):
                nc.tensor.transpose(PS[t // TPB][:, (t % TPB) * P:(t % TPB + 1) * P],
                                    m["X"][:, t * P:(t + 1) * P], m["ident"][:]).then_inc(fwd, 1)
            for t in range(TILES):
                pe.wait_ge(normed, t + 1)
                nc.tensor.transpose(PS[2 + t // TPB][:, (t % TPB) * P:(t % TPB + 1) * P],
                                    xn[:, t, :], m["ident"][:]).then_inc(back, 1)

        @block.vector
        def _(dve):
            for t in range(TILES):
                dve.wait_ge(fwd, (t // TPB + 1) * TPB)
                nc.vector.bn_stats(bst[:, t, :], PS[t // TPB][:, (t % TPB) * P:(t % TPB + 1) * P]).then_inc(stats.sem, 1)
            dve.wait_ge(stats.sem, stats.at(0, TILES))
            combine_stats(nc, dve, bst, mean, var, dif, stats, 0, TILES)
            rsqrt_ops(nc, dve, var[:], rstd[:], tmp[:], newton, 0, (EPS, 0.0))
            dve.wait_ge(newton.sem, newton.at(0))
            for t in range(TILES):
                nc.vector.tensor_scalar(xn[:, t, :], PS[t // TPB][:, (t % TPB) * P:(t % TPB + 1) * P],
                                        mean[:, t:t + 1], rstd[:, t:t + 1], ALU.subtract, ALU.mult).then_inc(normed, 1)

        @block.scalar
        def _(act):
            for b in range(B):
                act.wait_ge(back, (b + 1) * TPB)
                nc.scalar.activation(m["H"][:, b * SEQ + 1:(b + 1) * SEQ], PS[2 + b][:], ACT.Copy).then_inc(evac, 1)


def global_attention(nc, ins, m, kind):
    ctx = ExitStack()
    with ctx:
        def sb(name, shape, dt=FP32):
            return ctx.enter_context(nc.sbuf_tensor(f"{kind}_{name}", shape, dt))

        def sem(name):
            return m["sems"].enter_context(nc.semaphore(f"{kind}_{name}"))

        PS, X, H, ident, ident16 = m["PS"], m["X"], m["H"], m["ident"], m["ident16"]
        wq, wk, wv, wo = (sb(f"w{x}", [P, C]) for x in "qkvo")
        mask = sb("diag_mask", [P, P], BF16)
        V = sb("V", [P, TILES, C])
        Y = sb("Y", [P, TILES, C])
        qk_scr = nc.dram_tensor(f"{kind}_qk_scratch", [2, B, C, T], FP32).ap()
        w_in, qk_mm, qk_ev, v_mm, v_ev, qk_st = (sem(x) for x in (
            "weights_in", "qk_projected", "qk_evacuated", "v_projected", "v_evacuated", "qk_stored"))

        proj = ExitStack()
        with proj:
            qkT = proj.enter_context(nc.sbuf_tensor(f"{kind}_qkT", [P, 2, N], FP32))
            block = proj.enter_context(nc.Block())

            def hcols(b, off, n):
                return H[:, b * SEQ + 1 + off:b * SEQ + 1 + off + n]

            @block.sync
            def _(sp):
                for w, name in ((wq, "wq"), (wk, "wk"), (wv, "wv"), (wo, "wo")):
                    sp.dma_start(w[:], ins[kind + name]).then_inc(w_in, 16)
                sp.dma_start(mask[:], ins[kind + "mask"].bitcast(BF16)).then_inc(w_in, 16)
                for s in range(2):
                    sp.wait_ge(qk_ev, 2 * (s + 1))
                    sp.dma_start(qk_scr[s].rearrange("b c t -> c b t"),
                                 qkT[:, s, :].rearrange("c (b t) -> c b t", b=B)).then_inc(qk_st, 16)
                sp.wait_ge(qk_st, 32)

            @block.tensor
            def _(pe):
                pe.wait_ge(w_in, 80)
                for s, w in enumerate((wq, wk)):
                    for b in range(B):
                        for o in range(T // BLK):
                            nc.tensor.matmul(PS[2 * s + b][:, o * BLK:(o + 1) * BLK], w[:], hcols(b, o * BLK, BLK),
                                             start=True, stop=True).then_inc(qk_mm, 1)
                for t in range(TILES):
                    if t % TPB == 0:
                        pe.wait_ge(qk_ev, t // TPB + 1)
                    nc.tensor.matmul(PS[t // TPB][:, (t % TPB) * P:(t % TPB + 1) * P],
                                     hcols(t // TPB, (t % TPB) * P, P), wv[:], start=True, stop=True).then_inc(v_mm, 1)

            @block.scalar
            def _(act):
                for s in range(2):
                    for b in range(B):
                        act.wait_ge(qk_mm, 4 * s + 2 * (b + 1))
                        nc.scalar.activation(qkT[:, s, b * T:(b + 1) * T], PS[2 * s + b][:], ACT.Copy,
                                             scale=1.0 / math.sqrt(HD) if s == 0 else 1.0).then_inc(qk_ev, 1)
                for b in range(B):
                    act.wait_ge(v_mm, (b + 1) * TPB)
                    nc.scalar.activation(V[:, b * TPB:(b + 1) * TPB, :].rearrange("p t c -> p (t c)"), PS[b][:],
                                         ACT.Copy, scale=1e-3 if kind == "A" else 1.0).then_inc(v_ev, 1)

        if kind == "A":
            polymax_heads(nc, m, V, Y, mask, qk_scr)
        else:
            softmax_heads(nc, m, V, Y, mask, qk_scr)

        fin = ExitStack()
        with fin:
            yT = fin.enter_context(nc.sbuf_tensor(f"{kind}_yT", [P, N], FP32))
            y_tr, y_ev, o_mm, x_add = (sem(x) for x in (
                "y_transposed", "y_evacuated", "out_projected", "x_added"))
            block = fin.enter_context(nc.Block())

            @block.tensor
            def _(pe):
                for t in range(TILES):
                    nc.tensor.transpose(PS[t // TPB][:, (t % TPB) * P:(t % TPB + 1) * P], Y[:, t, :],
                                        ident[:]).then_inc(y_tr, 1)
                for b in range(B):
                    pe.wait_ge(y_ev, b + 1)
                    for o in range(T // BLK):
                        nc.tensor.matmul(PS[2 + b][:, o * BLK:(o + 1) * BLK], wo[:],
                                         yT[:, b * T + o * BLK:b * T + (o + 1) * BLK],
                                         start=True, stop=True).then_inc(o_mm, 1)

            @block.scalar
            def _(act):
                for b in range(B):
                    act.wait_ge(y_tr, (b + 1) * TPB)
                    nc.scalar.activation(yT[:, b * T:(b + 1) * T], PS[b][:], ACT.Copy).then_inc(y_ev, 1)

            @block.vector
            def _(dve):
                for b in range(B):
                    dve.wait_ge(o_mm, 2 * (b + 1))
                    nc.vector.tensor_tensor(X[:, b * T:(b + 1) * T], X[:, b * T:(b + 1) * T], PS[2 + b][:],
                                            ALU.add).then_inc(x_add, 1)


PAIRS = B * HEADS
UNITS = 2 * TPB


def load_heads(nc, sp, qk_scr, heads, in_sem, heads_used):
    flat = qk_scr.rearrange("s b c t -> s (b c t)")
    with sp.Fori(0, PAIRS // 2) as r:
        for u in range(2):
            at = nc.sync.snap((r * 2 + u) * (HD * T))
            sp.wait_ge(heads_used.sem, heads_used.at(r * 2 + u - 2))
            for s in range(2):
                sp.dma_start(heads[s][u][:], flat[s, bass.ds(at, HD * T)].rearrange("(d t) -> d t", d=HD))\
                    .then_inc(in_sem[u], 16)


def polymax_heads(nc, m, V, Y, mask, qk_scr):
    ctx = ExitStack()
    with ctx:
        def sb(name, shape, dt=FP32):
            return ctx.enter_context(nc.sbuf_tensor(f"poly_{name}", shape, dt))

        def sem(name):
            return m["sems"].enter_context(nc.semaphore(f"poly_{name}"))

        PS = m["PS"]
        heads = [[sb(f"{x}h{u}", [HD, T]) for u in range(2)] for x in "qk"]
        relu = [sb(f"relu{i}", [P, 1024]) for i in range(2)]
        line = [sb(f"line{i}", [P, 1024]) for i in range(2)]
        sqr = [sb(f"sqr{i}", [P, 1024]) for i in range(2)]
        F = [sb(f"F{i}", [P, 1024]) for i in range(2)]
        in_sem = [sem(f"head_in{u}") for u in range(2)]
        s_mm = Sig(sem("scores"), 1)
        relued = Sig(sem("relu_done"), 1)
        lined = Sig(sem("line_done"), 1, 1)
        squared = Sig(sem("square_done"), 1, 2)
        w_max = Sig(sem("max_done"), 1, 2)
        f_ready = Sig(sem("f_ready"), 1, 3)
        pv = Sig(sem("pv_done"), 1, 2)
        y_out = Sig(sem("y_written"), 1, 2)
        head_used = Sig(sem("head_used"), 1, 2)
        block = ctx.enter_context(nc.Block())
        full = lambda it: (it + 1) * P

        @block.sync
        def _(sp):
            load_heads(nc, sp, qk_scr, heads, in_sem, head_used)

        @block.tensor
        def _(pe):
            head_used.open(pe)
            pv.open(pe)

            def scores(r, s):
                u, it = s // TPB, s % TPB
                if it == 0:
                    pe.wait_ge(in_sem[u], r * 32 + 32)
                ps = PS[s % 3]
                pe.wait_ge(f_ready.sem, f_ready.at(r * UNITS + s - 3))
                for jt in range(it + 1):
                    mm = nc.tensor.matmul(ps[:, jt * P:(jt + 1) * P], heads[1][u][:, jt * P:(jt + 1) * P],
                                          heads[0][u][:, it * P:(it + 1) * P], start=True, stop=jt < it)
                if it == TPB - 1:
                    mm.then_inc(head_used.sem, 1)
                nc.tensor.matmul(ps[:, it * P:(it + 1) * P], m["ident16"][:], mask[:],
                                 start=False, stop=True).then_inc(s_mm.sem, 1)

            def product(r, s):
                u, it = s // TPB, s % TPB
                n = r * 2 + u
                if it == 0:
                    pe.wait_ge(y_out.sem, y_out.at(n - 2))
                pe.wait_ge(f_ready.sem, f_ready.at(r * UNITS + s))
                for jt in range(it + 1):
                    mm = nc.tensor.matmul(
                        PS[3][:, u * 512 + it * HD:u * 512 + (it + 1) * HD], F[s % 2][:, jt * P:(jt + 1) * P],
                        V[:, bass.ds(((n >> 4) & 1) * TPB + jt, 1), bass.ds((n & (HEADS - 1)) * HD, HD)].rearrange(
                            "p a d -> p (a d)"),
                        start=(jt == 0), stop=(jt == it))
                mm.then_inc(pv.sem, 1)

            with pe.Fori(0, PAIRS // 2) as r:
                for s in range(UNITS):
                    scores(r, s)
                    if s >= 1:
                        product(r, s - 1)
                product(r, UNITS - 1)

        @block.scalar
        def _(act):
            lined.open(act)
            with act.Fori(0, PAIRS // 2) as r:
                for s in range(UNITS):
                    n, it = r * UNITS + s, s % TPB
                    k = full(it)
                    act.wait_ge(s_mm.sem, s_mm.at(n))
                    act.wait_ge(squared.sem, squared.at(n - 2))
                    nc.scalar.activation(relu[s % 2][:, 0:k], PS[s % 3][:, 0:k], ACT.Relu).then_inc(relued.sem, 1)
                    act.wait_ge(w_max.sem, w_max.at(n - 2))
                    nc.scalar.activation(line[s % 2][:, 0:k], PS[s % 3][:, 0:k], ACT.Copy, scale=-0.01,
                                         bias=1.0).then_inc(lined.sem, 1)

        @block.gpsimd
        def _(pool):
            squared.open(pool)
            with pool.Fori(0, PAIRS // 2) as r:
                for s in range(UNITS):
                    n, k = r * UNITS + s, full(s % TPB)
                    pool.wait_ge(relued.sem, relued.at(n))
                    pool.wait_ge(w_max.sem, w_max.at(n - 2))
                    nc.gpsimd.tensor_tensor(sqr[s % 2][:, 0:k], relu[s % 2][:, 0:k], relu[s % 2][:, 0:k],
                                            ALU.mult).then_inc(squared.sem, 1)

        @block.vector
        def _(dve):
            w_max.open(dve)
            f_ready.open(dve)
            y_out.open(dve)

            with dve.Fori(0, PAIRS // 2) as r:
                for s in range(UNITS):
                    n, it, u = r * UNITS + s, s % TPB, s // TPB
                    k = full(it)
                    dve.wait_ge(squared.sem, squared.at(n))
                    dve.wait_ge(lined.sem, lined.at(n))
                    dve.wait_ge(pv.sem, pv.at(n - 2))
                    nc.vector.scalar_tensor_tensor(F[s % 2][:, 0:k], sqr[s % 2][:, 0:k], 1.0, line[s % 2][:, 0:k],
                                                   ALU.add, ALU.max).then_inc(w_max.sem, 1)
                    dve.wait_ge(w_max.sem, w_max.at(n))
                    nc.vector.scalar_tensor_tensor(F[s % 2][:, 0:k], PS[s % 3][:, 0:k], -100.0, F[s % 2][:, 0:k],
                                                   ALU.is_ge, ALU.mult).then_inc(f_ready.sem, 1)
                    if it == TPB - 1:
                        h = r * 2 + u
                        dve.wait_ge(pv.sem, pv.at(n))
                        nc.vector.tensor_copy(
                            Y[:, bass.ds(((h >> 4) & 1) * TPB, TPB), bass.ds((h & (HEADS - 1)) * HD, HD)],
                            heads_of(PS[3][:, u * 512:u * 512 + TPB * HD], TPB)).then_inc(y_out.sem, 1)


def softmax_heads(nc, m, V, Y, mask, qk_scr):
    ctx = ExitStack()
    with ctx:
        def sb(name, shape, dt=FP32):
            return ctx.enter_context(nc.sbuf_tensor(f"soft_{name}", shape, dt))

        def sem(name):
            return m["sems"].enter_context(nc.semaphore(f"soft_{name}"))

        PS = m["PS"]
        heads = [[sb(f"{x}h{u}", [HD, T]) for u in range(2)] for x in "qk"]
        E = [sb(f"E{i}", [P, 1024]) for i in range(2)]
        ET = [sb(f"ET{i}", [P, 1024]) for i in range(2)]
        nmx = sb("neg_max", [P, UNITS])
        rsum = sb("row_sum", [P, UNITS])
        rinv = sb("row_inverse", [P, UNITS])
        in_sem = [sem(f"head_in{u}") for u in range(2)]
        s_mm = Sig(sem("scores"), 1)
        maxed = Sig(sem("max_done"), 1)
        expd = Sig(sem("exp_done"), 1, 2)
        tr = Sig(sem("transposed"), 1, 2)
        ev = Sig(sem("evacuated"), 2, 1)
        pv = Sig(sem("pv_done"), 1, 2)
        inv = Sig(sem("inverse_done"), 1)
        y_out = Sig(sem("y_written"), 1, 2)
        head_used = Sig(sem("head_used"), 1, 2)
        block = ctx.enter_context(nc.Block())
        full = lambda it: (it + 1) * P
        half = lambda it: (it + 1) // 2 * P if it < 5 else 512

        @block.sync
        def _(sp):
            load_heads(nc, sp, qk_scr, heads, in_sem, head_used)

        @block.tensor
        def _(pe):
            head_used.open(pe)
            tr.open(pe)
            pv.open(pe)

            def scores(r, s):
                u, it = s // TPB, s % TPB
                if it == 0:
                    pe.wait_ge(in_sem[u], r * 32 + 32)
                pe.wait_ge(expd.sem, expd.at(r * UNITS + s - 2))
                ps = PS[s % 2]
                k = full(it)
                for o in range(0, k, BLK):
                    e = min(k, o + BLK)
                    mm = nc.tensor.matmul(ps[:, o:e], heads[0][u][:, it * P:(it + 1) * P], heads[1][u][:, o:e],
                                          start=True, stop=e < k)
                if it == TPB - 1:
                    mm.then_inc(head_used.sem, 1)
                nc.tensor.matmul(ps[:, it * P:(it + 1) * P], m["ident16"][:], mask[:],
                                 start=False, stop=True).then_inc(s_mm.sem, 1)

            def transposes(r, s):
                it = s % TPB
                pe.wait_ge(expd.sem, expd.at(r * UNITS + s))
                pe.wait_ge(ev.sem, ev.at(r * UNITS + s - 1))
                for jt in range(it + 1):
                    mm = nc.tensor.transpose(PS[2][:, jt * P:(jt + 1) * P], E[s % 2][:, jt * P:(jt + 1) * P],
                                             m["ident"][:])
                mm.then_inc(tr.sem, 1)

            def product(r, s):
                u, it = s // TPB, s % TPB
                n = r * 2 + u
                if it == 0:
                    pe.wait_ge(y_out.sem, y_out.at(n - 2))
                pe.wait_ge(ev.sem, ev.at(r * UNITS + s))
                for jt in range(it + 1):
                    mm = nc.tensor.matmul(
                        PS[3][:, u * 512 + it * HD:u * 512 + (it + 1) * HD], ET[s % 2][:, jt * P:(jt + 1) * P],
                        V[:, bass.ds(((n >> 4) & 1) * TPB + jt, 1), bass.ds((n & (HEADS - 1)) * HD, HD)].rearrange(
                            "p a d -> p (a d)"),
                        start=(jt == 0), stop=(jt == it))
                mm.then_inc(pv.sem, 1)

            with pe.Fori(0, PAIRS // 2) as r:
                for s in range(UNITS):
                    scores(r, s)
                    if s >= 2:
                        product(r, s - 2)
                    if s >= 1:
                        transposes(r, s - 1)
                transposes(r, UNITS - 1)
                product(r, UNITS - 2)
                product(r, UNITS - 1)

        @block.scalar
        def _(act):
            expd.open(act)

            def evacuate(r, s):
                it, n = s % TPB, r * UNITS + s
                act.wait_ge(tr.sem, tr.at(n))
                act.wait_ge(pv.sem, pv.at(n - 2))
                c = half(it)
                if c:
                    ins = nc.scalar.activation(ET[s % 2][:, 0:c], PS[2][:, 0:c], ACT.Copy)
                    ins.then_inc(ev.sem, 1)

            with act.Fori(0, PAIRS // 2) as r:
                for s in range(UNITS):
                    n, k = r * UNITS + s, full(s % TPB)
                    act.wait_ge(maxed.sem, maxed.at(n))
                    act.wait_ge(tr.sem, tr.at(n - 2))
                    nc.scalar.activation(E[s % 2][:, 0:k], PS[s % 2][:, 0:k], ACT.Exp, bias=nmx[:, s:s + 1],
                                         accum_out=rsum[:, s:s + 1]).then_inc(expd.sem, 1)
                    if s >= 1:
                        evacuate(r, s - 1)
                evacuate(r, UNITS - 1)

        @block.vector
        def _(dve):
            ev.open(dve)
            y_out.open(dve)

            def evacuate(r, s):
                it, n = s % TPB, r * UNITS + s
                c, k = half(it), full(it)
                dve.wait_ge(tr.sem, tr.at(n))
                dve.wait_ge(pv.sem, pv.at(n - 2))
                if c < 512:
                    if c:
                        dve.wait_ge(ev.sem, ev.at(n, 1))
                ins = nc.vector.tensor_copy(ET[s % 2][:, c:k], PS[2][:, c:k])
                ins.then_inc(ev.sem, 1 if c else 2)

            def finish(r, u):
                h = r * 2 + u
                cols = slice(u * TPB, (u + 1) * TPB)
                dve.wait_ge(expd.sem, expd.at(r * UNITS + u * TPB + TPB - 1))
                nc.vector.reciprocal(rinv[:, cols], rsum[:, cols]).then_inc(inv.sem, 1)
                dve.wait_ge(inv.sem, inv.at(h))
                dve.wait_ge(pv.sem, pv.at(r * UNITS + u * TPB + TPB - 1))
                nc.vector.tensor_tensor(
                    Y[:, bass.ds(((h >> 4) & 1) * TPB, TPB), bass.ds((h & (HEADS - 1)) * HD, HD)],
                    heads_of(PS[3][:, u * 512:u * 512 + TPB * HD], TPB), over(rinv[:, cols], HD),
                    ALU.mult).then_inc(y_out.sem, 1)

            with dve.Fori(0, PAIRS // 2) as r:
                for s in range(UNITS):
                    n, k = r * UNITS + s, full(s % TPB)
                    dve.wait_ge(s_mm.sem, s_mm.at(n))
                    nc.vector.tensor_reduce(nmx[:, s:s + 1], PS[s % 2][:, 0:k], AX.X, ALU.max,
                                            negate=True).then_inc(maxed.sem, 1)
                    if s >= 1:
                        evacuate(r, s - 1)
                    if s == TPB + 1:
                        finish(r, 0)
                evacuate(r, UNITS - 1)
                finish(r, 1)


def ffn_stack(nc, ins, m, call):
    ctx = ExitStack()
    tag = f"f{call}"
    first = call * DEPTH
    with ctx:
        def sb(name, shape, dt=FP32):
            return ctx.enter_context(nc.sbuf_tensor(f"{tag}_{name}", shape, dt))

        def sig(name, per=1, credit=0):
            if name not in m["stack"]:
                m["stack"][name] = Sig(m["sems"].enter_context(nc.semaphore(f"stack_{name}")), per, credit)
            return m["stack"][name]

        PS, X, H, G, ident, ident16 = (m[k] for k in ("PS", "X", "H", "G", "ident", "ident16"))
        wqkv = sb("wqkv", [P, 3 * INNER])
        wo = sb("wo", [P, HP, C])
        w1 = sb("w1", [P, 2 * DI])
        w2 = sb("w2", [P, 3, C])
        b1 = sb("b1", [P, 6])
        vec = sb("ln_g_ln_b_b2", [P, 3])
        qks = sb("qk_scales", [P, 4, DH])
        rope0 = sb("rope_base", [P, 4, TPB, DH])
        rope = sb("rope", [P, 4, TPB, DH])
        mask = sb("band_mask", [P, TPB, 2 * W], BF16)
        keep = sb("keep_previous", [P, TPB])
        xs = [sb(f"xs{u}", [P, P]) for u in range(2)]
        sq = [sb(f"sq{x}", [P, INNER]) for x in "qk"]
        ss = sb("sum_of_squares", [P, 2 * HEADS])
        rn = sb("inverse_norm", [P, 2 * HEADS])
        rt = sb("rsqrt_tmp", [P, 2 * HEADS])
        ra = [sb(f"rope_a{x}", [P, INNER]) for x in "qk"]
        rb = [sb(f"rope_b{x}", [P, INNER]) for x in "qk"]
        qk = [sb(f"{x}_rotated", [P, INNER]) for x in "qk"]
        qT = sb("qT", [P, HP, P])
        kT = [sb(f"kT{u}", [P, HP, W + P]) for u in range(2)]
        V = [sb(f"V{u}", [P, INNER]) for u in range(2)]
        mx = sb("row_max", [P, HEADS])
        sd = sb("shifted", [P, INNER])
        E = sb("E", [P, INNER])
        rs = sb("row_sum", [P, HEADS])
        ri = sb("row_inverse", [P, HEADS])
        PB = sb("P_banded", [P, HEADS, P])
        PP = sb("P_previous", [W, HEADS, W])
        PPT = sb("P_previous_T", [P, HEADS, W])
        PT = sb("P_T", [P, HEADS, P])
        OT = sb("O_T", [P, HP, P])
        gs = [sb(f"gs{i}", [P, BLK]) for i in range(2)]
        bst = sb("bn_stats", [P, TB, 6])
        mean, dif = sb("mean", [P, TB]), sb("mean_gap", [P, TB])
        var = sb("var", [P, TB])
        rstd = sb("rstd", [P, TB])
        rt2 = sb("rsqrt_tmp2", [P, TB])
        xn = sb("xn", [P, TB, C])
        xnT = sb("xnT", [P, BLK])
        ge = [sb(f"gelu{j}", [P, BLK]) for j in range(3)]
        hm = [sb(f"hidden{j}", [P, BLK]) for j in range(3)]

        consts = sig("consts_in", 48)
        wqkv_in, wo_in, ffn_in, qks_in = sig("wqkv_in", 16), sig("wo_in", 16), sig("ffn_w_in", 16 * 14), \
            sig("qk_scales_in", 96)
        cleared = sig("cleared", 4)
        rope_t = sig("rope_tables", 4)
        xs_t = sig("xs_ready", 2)
        q_mm, k_mm, v_mm = sig("q_projected"), sig("k_projected"), sig("v_projected", 1, 2)
        sqd = sig("squared", 2)
        red = sig("reduced", 2, 1)
        newton = sig("qk_rsqrt_steps", RSQRT_STEPS)
        rot = sig("rope_products", 6, 1)
        rsum = sig("rope_added", 2)
        nrm = sig("qk_normalised", 2, 1)
        qT_mm, kT_mm = sig("q_transposed", 1, 1), sig("k_transposed", 1, 1)
        qT_ev, kT_ev = sig("qT_evacuated"), sig("kT_evacuated", 2)
        s_mm = sig("scores")
        mxd, sbd, expd, smd, rid = sig("max_done"), sig("shift_done"), sig("exp_done", 1, 1), \
            sig("sum_done"), sig("inverse_done")
        spread = sig("P_spread", 5, 1)
        ppt = sig("P_previous_transposed", 1, 1)
        pt_mm, pt_ev = sig("P_transposed", 2, 1), sig("PT_evacuated", 2, 1)
        o_mm, o_ev, v_ev, y_mm, g_add = sig("o_done", 1, 1), sig("o_evacuated", 1, 1), sig("v_evacuated"), \
            sig("y_done", 1, 1), sig("g_added", 1, 1)
        gs_t, f_tr, f_st, f_nt = sig("gs_ready", 2), sig("g_to_tokens", 1), sig("stats", 7), \
            sig("ffn_rsqrt_steps", RSQRT_STEPS)
        f_xn, f_bk, f_xnT = sig("xn_ready", 1), sig("xn_to_channels", 1), sig("xnT_ready", 1, 1)
        f_h, f_ge, f_hm = sig("hidden_done", 3), sig("gelu_done", 3), sig("gated_done", 3, 1)
        f_y, f_t2, h_new = sig("ffn_out_done", 1, 1), sig("ffn_residual", 1), sig("h_written", 1, 1)
        x_add = sig("x_added", 2)
        block = ctx.enter_context(nc.Block())

        def pair(u, job):
            return PS[(10 * (u % 2) + job) % 4]

        JQT, JKT, JS, JQ, JK, JV, JP0, JP1, JO, JY = range(10)

        @block.sync
        def _(sp):
            sp.dma_start(rope0[:], ins["rope"]).then_inc(consts.sem, 16)
            sp.dma_start(mask[:], ins["band"].bitcast(BF16)).then_inc(consts.sem, 16)
            sp.dma_start(keep[:], ins["keep"]).then_inc(consts.sem, 16)
            with sp.Fori(0, DEPTH) as layer:
                l = layer + first
                def of_layer(name):
                    ap = ins[name]
                    size = int(np.prod(ap.shape[1:]))
                    flat = ap.rearrange("l c n -> (l c n)" if len(ap.shape) == 3 else "l n -> (l n)")
                    part = flat[bass.ds(nc.sync.snap(layer * size), size)]
                    return part.rearrange("(c n) -> c n", n=ap.shape[2]) if len(ap.shape) == 3 else \
                        part.rearrange("(a n) -> a n", a=1)

                par = {k: of_layer(k) for k in FFN_PARAMS}
                sp.wait_ge(v_mm.sem, v_mm.at(l * TILES - 1))
                sp.dma_start(wqkv[:], par["L0_ffn_Wqkv"])\
                    .then_inc(wqkv_in.sem, 16)
                sp.wait_ge(rot.sem, rot.at(l * TILES - 1))
                qs, ks = (par[x].to_broadcast([P, DH]) for x in
                          ("L0_ffn_q_scale", "L0_ffn_k_scale"))
                hh = DH // 2
                for i, s in enumerate((qs, ks)):
                    sp.dma_start(qks[:, 2 * i, :], s).then_inc(qks_in.sem, 16)
                    sp.dma_start(qks[:, 2 * i + 1, 0:hh], s[:, hh:DH]).then_inc(qks_in.sem, 16)
                    sp.dma_start(qks[:, 2 * i + 1, hh:DH], s[:, 0:hh]).then_inc(qks_in.sem, 16)
                sp.wait_ge(y_mm.sem, y_mm.at(l * TILES - 1))
                sp.dma_start(wo[:], par["L0_ffn_Wo"].rearrange("(k p) c -> p k c", p=P))\
                    .then_inc(wo_in.sem, 16)
                sp.wait_ge(h_new.sem, h_new.at(l * NBLK - 1))
                f = ffn_in.sem
                sp.dma_start(w1[:], par["L0_ffn_W1"]).then_inc(f, 16)
                for j, (o, k) in enumerate(FCH):
                    sp.dma_start(w2[0:k, j, :], par["L0_ffn_W2"][o:o + k, :]).then_inc(f, 16)
                    for g in range(2):
                        sp.dma_start(b1[0:k, 3 * g + j:3 * g + j + 1],
                                     par["L0_ffn_b1"][:, g * DI + o:g * DI + o + k].rearrange("a k -> k a")).then_inc(f, 16)
                for i, x in enumerate(("L0_ffn_ln_g", "L0_ffn_ln_b", "L0_ffn_b2")):
                    sp.dma_start(vec[:, i:i + 1], par[x].rearrange("a k -> k a")).then_inc(f, 16)
                sp.sem_inc(f, 16)

        @block.tensor
        def _(pe):
            if call == 0:
                for s in (v_mm, qT_mm, kT_mm, pt_mm, o_mm, y_mm, f_y):
                    s.open(pe)

            def project_first(l, n):
                pe.wait_ge(wqkv_in.sem, wqkv_in.at(l))
                pe.wait_ge(h_new.sem, h_new.at(l * NBLK - 1))
                pe.wait_ge(xs_t.sem, xs_t.at(n))
                for job, s, c in ((JQ, q_mm, 0), (JK, k_mm, 1), (JV, v_mm, 2)):
                    ps = pair(1, job)
                    for o in range(2):
                        mm = nc.tensor.matmul(ps[:, o * 512:(o + 1) * 512], xs[0][:],
                                              wqkv[:, c * INNER + o * 512:c * INNER + (o + 1) * 512],
                                              start=True, stop=True)
                    mm.then_inc(s.sem, 1)

            def project_next(n, u):
                pe.wait_ge(xs_t.sem, xs_t.at(n + 1))
                for job, s, c, read, of in ((JQ, q_mm, 0, g_add, n - 1), (JK, k_mm, 1, qT_ev, n),
                                            (JV, v_mm, 2, kT_ev, n)):
                    pe.wait_ge(read.sem, read.at(of))
                    for o in range(2):
                        mm = nc.tensor.matmul(pair(u, job)[:, o * 512:(o + 1) * 512], xs[1 - u][:],
                                              wqkv[:, c * INNER + o * 512:c * INNER + (o + 1) * 512],
                                              start=True, stop=True)
                    mm.then_inc(s.sem, 1)

            def attend(n, p, u, last):
                for i, (job, s) in enumerate(((JQT, qT_mm), (JKT, kT_mm))):
                    pe.wait_ge(nrm.sem, nrm.at(n, i + 1))
                    pe.wait_ge(pt_ev.sem, pt_ev.at(n - 1, i + 1))
                    for k in range(HP):
                        mm = nc.tensor.transpose(pair(u, job)[:, k * P:(k + 1) * P], qk[i][:, k * P:(k + 1) * P],
                                                 ident[:])
                    mm.then_inc(s.sem, 1)
                pe.wait_ge(o_ev.sem, o_ev.at(n - 1))
                S = pair(u, JS)
                pe.wait_ge(qT_ev.sem, qT_ev.at(n))
                pe.wait_ge(kT_ev.sem, kT_ev.at(n))
                for i in range(2):
                    nc.tensor.matmul(S[:, i * 512:(i + 1) * 512], ident16[:],
                                     mask[:, bass.ds(tile_of(p, u), 1), :].to_broadcast([P, HP, 2 * W]),
                                     start=True, stop=False)
                for k in range(HP):
                    for i in range(2):
                        rows = slice(i * DH, (i + 1) * DH)
                        for g in range(NG):
                            c = i * 512 + k * 2 * W
                            mm = nc.tensor.matmul(
                                S[g * W:(g + 1) * W, c:c + 2 * W], qT[rows, k, g * W:(g + 1) * W],
                                kT[u][rows, k, g * W:(g + 2) * W], start=False, stop=k == HP - 1)
                mm.then_inc(s_mm.sem, 1)
                if not last:
                    project_next(n, u)
                pe.wait_ge(spread.sem, spread.at(n))
                for half in range(2):
                    if half == 0:
                        pe.wait_ge(sbd.sem, sbd.at(n))
                    elif not last:
                        pe.wait_ge(sqd.sem, sqd.at(n + 1, 1))
                        pe.wait_ge(rot.sem, rot.at(n + 1, 3))
                    for k in range(HP):
                        mm = nc.tensor.transpose(pair(u, JP0 + half)[:, k * P:(k + 1) * P], PB[:, half * HP + k, :],
                                                 ident[:])
                    mm.then_inc(pt_mm.sem, 1)
                if not last:
                    pe.wait_ge(sqd.sem, sqd.at(n + 1, 2))
                    pe.wait_ge(rot.sem, rot.at(n + 1, 6))
                pe.wait_ge(ppt.sem, ppt.at(n))
                pe.wait_ge(v_ev.sem, v_ev.at(n))
                pe.wait_ge(pt_ev.sem, pt_ev.at(n))
                for h in range(HEADS):
                    k, i = h // 2, h % 2
                    O = pair(u, JO)
                    rows = slice(i * DH, (i + 1) * DH)
                    nc.tensor.matmul(O[rows, k * P:(k + 1) * P], V[u][:, h * DH:(h + 1) * DH], PT[:, h, :],
                                     start=True, stop=False)
                    mm = nc.tensor.matmul(O[rows, k * P:k * P + W], V[1 - u][P - W:P, h * DH:(h + 1) * DH],
                                          PPT[P - W:P, h, :], start=False, stop=True)
                mm.then_inc(o_mm.sem, 1)
                pe.wait_ge(o_ev.sem, o_ev.at(n))
                if not last:
                    pe.wait_ge(v_ev.sem, v_ev.at(n + 1))
                for k in range(HP):
                    mm = nc.tensor.matmul(pair(u, JY)[:, 0:P], wo[:, k, :], OT[:, k, :], start=(k == 0),
                                          stop=(k == HP - 1))
                mm.then_inc(y_mm.sem, 1)

            def feed(l, b):
                n = l * NBLK + b
                pe.wait_ge(gs_t.sem, gs_t.at(n))
                if b == 0:
                    pe.wait_ge(g_add.sem, g_add.at((l + 1) * TILES - 1))
                    pe.wait_ge(ffn_in.sem, ffn_in.at(l))
                for t in range(TB):
                    mm = nc.tensor.transpose(PS[0][:, t * P:(t + 1) * P], gs[b % 2][:, t * P:(t + 1) * P], ident[:])
                mm.then_inc(f_tr.sem, 1)
                pe.wait_ge(f_xn.sem, f_xn.at(n))
                pe.wait_ge(h_new.sem, h_new.at(n - 1))
                for t in range(TB):
                    mm = nc.tensor.transpose(PS[0][:, 512 + t * P:512 + (t + 1) * P], xn[:, t, :], ident[:])
                mm.then_inc(f_bk.sem, 1)
                pe.wait_ge(f_xnT.sem, f_xnT.at(n))
                for j, (o, k) in enumerate(FCH):
                    pe.wait_ge(f_hm.sem, f_hm.at(n - 1, j + 1))
                    for g in range(2):
                        mm = nc.tensor.matmul(PS[1 + j][0:k, g * 512:(g + 1) * 512],
                                              w1[:, g * DI + o:g * DI + o + k], xnT[:], start=True, stop=True)
                    mm.then_inc(f_h.sem, 1)
                for j, (o, k) in enumerate(FCH):
                    pe.wait_ge(f_hm.sem, f_hm.at(n, j + 1))
                    mm = nc.tensor.matmul(PS[0][:, 512:1024], w2[0:k, j, :], hm[j][0:k, :], start=(j == 0),
                                          stop=(j == 2))
                mm.then_inc(f_y.sem, 1)

            pe.wait_ge(cleared.sem, cleared.at(call))
            pe.wait_ge(consts.sem, consts.at(call))
            with pe.Fori(first, first + DEPTH) as l:
                pe.wait_ge(wo_in.sem, wo_in.at(l))
                project_first(l, l * TILES)
                with pe.Fori(0, TPB - 1) as p:
                    for u in range(2):
                        attend(l * TILES + p * 2 + u, p, u, False)
                attend(l * TILES + TILES - 2, TPB - 1, 0, False)
                attend(l * TILES + TILES - 1, TPB - 1, 1, True)
                for b in range(NBLK):
                    feed(l, b)

        @block.scalar
        def _(act):
            if call == 0:
                for s in (expd, pt_ev, o_ev, f_xnT):
                    s.open(act)

            def shifted(n, p, u):
                off = tile_col(p, u)
                act.wait_ge(v_mm.sem, v_mm.at(n - 2))
                nc.scalar.activation(xs[u][0:64, :], H[0:64, bass.ds(off + 1, P)], ACT.Copy).then_inc(xs_t.sem, 1)
                nc.scalar.activation(xs[u][64:128, :], H[64:128, bass.ds(off, P)], ACT.Copy).then_inc(xs_t.sem, 1)

            def squares(n, u_pair):
                for i, s in enumerate((q_mm, k_mm)):
                    act.wait_ge(s.sem, s.at(n))
                    act.wait_ge(red.sem, red.at(n - 1, i + 1))
                    nc.scalar.activation(sq[i][:], pair(u_pair, JQ + i)[:], ACT.Square).then_inc(sqd.sem, 1)

            def values(n, u_pair, u):
                act.wait_ge(v_mm.sem, v_mm.at(n))
                nc.scalar.activation(V[u][:], pair(u_pair, JV)[:], ACT.Copy).then_inc(v_ev.sem, 1)

            def attend(n, p, u, last):
                if not last:
                    shifted(n + 1, p if u == 0 else p + 1, 1 - u)
                act.wait_ge(qT_mm.sem, qT_mm.at(n))
                nc.scalar.activation(qT[:].rearrange("p k t -> p (k t)"), pair(u, JQT)[:], ACT.Copy)\
                    .then_inc(qT_ev.sem, 1)
                act.wait_ge(kT_mm.sem, kT_mm.at(n))
                src = pair(u, JKT)[:].rearrange("p (k t) -> p k t", k=HP)
                nc.scalar.activation(kT[u][:, :, W:W + P], src, ACT.Copy).then_inc(kT_ev.sem, 1)
                nc.scalar.activation(kT[1 - u][:, :, 0:W], src[:, :, P - W:P], ACT.Copy,
                                     scale=keep[:, bass.ds(tile_of(p, u), 1)]).then_inc(kT_ev.sem, 1)
                act.wait_ge(sbd.sem, sbd.at(n))
                act.wait_ge(spread.sem, spread.at(n - 1))
                nc.scalar.activation(E[:], sd[:], ACT.Exp).then_inc(expd.sem, 1)
                if not last:
                    squares(n + 1, u)
                for half in range(2):
                    act.wait_ge(pt_mm.sem, pt_mm.at(n, half + 1))
                    act.wait_ge(o_mm.sem, o_mm.at(n - 1))
                    nc.scalar.activation(PT[:, half * HP:(half + 1) * HP, :].rearrange("p h t -> p (h t)"),
                                         pair(u, JP0 + half)[:], ACT.Copy).then_inc(pt_ev.sem, 1)
                act.wait_ge(o_mm.sem, o_mm.at(n))
                act.wait_ge(y_mm.sem, y_mm.at(n - 1))
                nc.scalar.activation(OT[:].rearrange("p k t -> p (k t)"), pair(u, JO)[:], ACT.Copy)\
                    .then_inc(o_ev.sem, 1)
                if not last:
                    values(n + 1, u, 1 - u)

            def feed(l, b):
                n = l * NBLK + b
                act.wait_ge(f_bk.sem, f_bk.at(n))
                if b:
                    act.wait_ge(f_h.sem, f_h.at(n - 1))
                nc.scalar.activation(xnT[:], PS[0][:, 512:1024], ACT.Identity, scale=vec[:, 0:1],
                                     bias=vec[:, 1:2]).then_inc(f_xnT.sem, 1)
                for j, (o, k) in enumerate(FCH):
                    act.wait_ge(f_h.sem, f_h.at(n, j + 1))
                    act.wait_ge(f_hm.sem, f_hm.at(n - 1, j + 1))
                    nc.scalar.activation(ge[j][0:k, :], PS[1 + j][0:k, 512:1024], ACT.Gelu,
                                         bias=b1[0:k, 3 + j:4 + j]).then_inc(f_ge.sem, 1)

            act.wait_ge(cleared.sem, cleared.at(call))
            act.wait_ge(consts.sem, consts.at(call))
            with act.Fori(first, first + DEPTH) as l:
                act.wait_ge(h_new.sem, h_new.at(l * NBLK - 1))
                shifted(l * TILES, 0, 0)
                squares(l * TILES, 1)
                values(l * TILES, 1, 0)
                with act.Fori(0, TPB - 1) as p:
                    for u in range(2):
                        attend(l * TILES + p * 2 + u, p, u, False)
                attend(l * TILES + TILES - 2, TPB - 1, 0, False)
                attend(l * TILES + TILES - 1, TPB - 1, 1, True)
                act.wait_ge(ffn_in.sem, ffn_in.at(l))
                for b in range(NBLK):
                    feed(l, b)

        @block.gpsimd
        def _(pool):
            if call == 0:
                spread.open(pool)
                nrm.open(pool)

            def rotate(n):
                pool.wait_ge(spread.sem, spread.at(n - 1))
                for i in range(2):
                    pool.wait_ge(rot.sem, rot.at(n, 3 * (i + 1)))
                    nc.gpsimd.tensor_tensor(ra[i][:], ra[i][:], rb[i][:], ALU.add).then_inc(rsum.sem, 1)
                pool.wait_ge(newton.sem, newton.at(n))
                for i, s in enumerate((qT_mm, kT_mm)):
                    pool.wait_ge(rsum.sem, rsum.at(n, i + 1))
                    pool.wait_ge(s.sem, s.at(n - 1))
                    nc.gpsimd.tensor_tensor(heads_of(qk[i][:]), heads_of(ra[i][:]),
                                            over(rn[:, i * HEADS:(i + 1) * HEADS], DH),
                                            ALU.mult).then_inc(nrm.sem, 1)

            def place(n):
                pool.wait_ge(nrm.sem, nrm.at(n))
                pool.wait_ge(rid.sem, rid.at(n))
                pool.wait_ge(expd.sem, expd.at(n))
                Ev = E[:].rearrange("p (i k j) -> p k i j", i=2, k=HP)
                Rv = ri[:].rearrange("p (i k) -> p k i", i=2)

                def norm(j, g, dst, j0, j1):
                    if j:
                        pool.wait_ge(spread.sem, spread.at(n, j))
                    r = slice(g * W, (g + 1) * W)
                    for_k = Rv[r].unsqueeze(3).to_broadcast([W, HP, 2, j1 - j0])
                    nc.gpsimd.tensor_tensor(dst.rearrange("p (k i) j -> p k i j", i=2), Ev[r, :, :, j0:j1], for_k,
                                            ALU.mult).then_inc(spread.sem, 1)

                pool.wait_ge(ppt.sem, ppt.at(n - 1))
                norm(0, 0, PP[:], 0, W)
                pool.wait_ge(pt_mm.sem, pt_mm.at(n - 1))
                norm(1, 0, PB[0:W, :, 0:W], W, 2 * W)
                for g in range(1, NG):
                    norm(g + 1, g, PB[g * W:(g + 1) * W, :, (g - 1) * W:(g + 1) * W], 0, 2 * W)

            nc.gpsimd.memset(PB[:], 0.0).then_inc(cleared.sem, 1)
            nc.gpsimd.memset(kT[0][:, :, 0:W], 0.0).then_inc(cleared.sem, 1)
            nc.gpsimd.memset(V[1][:], 0.0).then_inc(cleared.sem, 1)
            pool.sem_inc(cleared.sem, 1)
            pool.wait_ge(cleared.sem, cleared.at(call))
            with pool.Fori(first, first + DEPTH) as l:
                rotate(l * TILES)
                with pool.Fori(0, TILES - 1) as t:
                    place(l * TILES + t)
                    rotate(l * TILES + t + 1)
                place(l * TILES + TILES - 1)

        @block.vector
        def _(dve):
            if call == 0:
                for s in (red, rot, ppt, g_add, f_hm, h_new):
                    s.open(dve)

            def rotate(n, p, u, u_pair):
                tile = tile_of(p, u)
                for i, s in enumerate((q_mm, k_mm)):
                    dve.wait_ge(s.sem, s.at(n))
                    dve.wait_ge(sqd.sem, sqd.at(n, i + 1))
                    dve.wait_ge(nrm.sem, nrm.at(n - 1, i + 1))
                    src = heads_of(pair(u_pair, JQ + i)[:])
                    hh = DH // 2

                    def table(which, a, b):
                        return rope[:, which, bass.ds(tile, 1), a:b].to_broadcast([P, HEADS, b - a])

                    nc.vector.tensor_tensor(heads_of(ra[i][:]), src, table(2 * i, 0, DH), ALU.mult)\
                        .then_inc(rot.sem, 1)
                    nc.vector.tensor_tensor(heads_of(rb[i][:])[:, :, 0:hh], src[:, :, hh:DH],
                                            table(2 * i + 1, 0, hh), ALU.mult).then_inc(rot.sem, 1)
                    nc.vector.tensor_tensor(heads_of(rb[i][:])[:, :, hh:DH], src[:, :, 0:hh],
                                            table(2 * i + 1, hh, DH), ALU.mult).then_inc(rot.sem, 1)
                for i in range(2):
                    nc.vector.tensor_reduce(ss[:, i * HEADS:(i + 1) * HEADS], heads_of(sq[i][:]), AX.X, ALU.add)\
                        .then_inc(red.sem, 1)
                dve.wait_ge(red.sem, red.at(n))
                rsqrt_ops(nc, dve, ss[:], rn[:], rt[:], newton, n, (0.0, 1e-24))

            def soften(n, u):
                dve.wait_ge(s_mm.sem, s_mm.at(n))
                S = pair(u, JS)[:]
                nc.vector.tensor_reduce(mx[:], heads_of(S), AX.X, ALU.max).then_inc(mxd.sem, 1)
                dve.wait_ge(mxd.sem, mxd.at(n))
                dve.wait_ge(expd.sem, expd.at(n - 1))
                nc.vector.tensor_tensor(heads_of(sd[:]), heads_of(S), over(mx[:], DH), ALU.subtract)\
                    .then_inc(sbd.sem, 1)
                dve.wait_ge(expd.sem, expd.at(n))
                nc.vector.tensor_reduce(rs[:], heads_of(E[:]), AX.X, ALU.add).then_inc(smd.sem, 1)
                dve.wait_ge(smd.sem, smd.at(n))
                dve.wait_ge(spread.sem, spread.at(n - 1))
                nc.vector.reciprocal(ri[:], rs[:]).then_inc(rid.sem, 1)

            def finish(n, p, u):
                dve.wait_ge(spread.sem, spread.at(n, 1))
                dve.wait_ge(o_mm.sem, o_mm.at(n - 1))
                nc.vector.transpose(PPT[P - W:P].rearrange("p h q -> p (h q)"), PP[:].rearrange("p h q -> p (h q)"))\
                    .then_inc(ppt.sem, 1)
                dve.wait_ge(y_mm.sem, y_mm.at(n))
                off = tile_col(p, u) + 1
                nc.vector.tensor_tensor(G[:, bass.ds(off, P)], pair(u, JY)[:, 0:P], H[:, bass.ds(off, P)], ALU.add)\
                    .then_inc(g_add.sem, 1)

            def feed(l, b):
                n = l * NBLK + b
                q, o = b // 2, b % 2
                base = q * SEQ + o * BLK
                if b >= 2:
                    dve.wait_ge(f_tr.sem, f_tr.at(n - 2))
                if b == 0:
                    dve.wait_ge(g_add.sem, g_add.at((l + 1) * TILES - 1))
                nc.vector.tensor_copy(gs[b % 2][0:64, :], G[0:64, base + 1:base + 1 + BLK]).then_inc(gs_t.sem, 1)
                nc.vector.tensor_copy(gs[b % 2][64:128, :], G[64:128, base:base + BLK]).then_inc(gs_t.sem, 1)
                dve.wait_ge(f_tr.sem, f_tr.at(n))
                for t in range(TB):
                    ins_ = nc.vector.bn_stats(bst[:, t, :], PS[0][:, t * P:(t + 1) * P])
                ins_.then_inc(f_st.sem, 1)
                dve.wait_ge(f_st.sem, f_st.at(n, 1))
                combine_stats(nc, dve, bst, mean, var, dif, f_st, n, 1)
                rsqrt_ops(nc, dve, var[:], rstd[:], rt2[:], f_nt, n, (EPS, 0.0))
                dve.wait_ge(f_nt.sem, f_nt.at(n))
                if b:
                    dve.wait_ge(f_bk.sem, f_bk.at(n - 1))
                for t in range(TB):
                    ins_ = nc.vector.tensor_scalar(xn[:, t, :], PS[0][:, t * P:(t + 1) * P], mean[:, t:t + 1],
                                                   rstd[:, t:t + 1], ALU.subtract, ALU.mult)
                ins_.then_inc(f_xn.sem, 1)
                for j, (_, k) in enumerate(FCH):
                    dve.wait_ge(f_ge.sem, f_ge.at(n, j + 1))
                    dve.wait_ge(f_y.sem, f_y.at(n - 1))
                    nc.vector.scalar_tensor_tensor(hm[j][0:k, :], PS[1 + j][0:k, 0:512], b1[0:k, j:j + 1],
                                                   ge[j][0:k, :], ALU.add, ALU.mult).then_inc(f_hm.sem, 1)
                dve.wait_ge(f_y.sem, f_y.at(n))
                nc.vector.scalar_tensor_tensor(H[:, base + 1:base + 1 + BLK], PS[0][:, 512:1024], vec[:, 2:3],
                                               G[:, base + 1:base + 1 + BLK], ALU.add, ALU.add)\
                    .then_inc(h_new.sem, 1)

            dve.wait_ge(cleared.sem, cleared.at(call))
            dve.wait_ge(consts.sem, consts.at(call))
            with dve.Fori(first, first + DEPTH) as l:
                dve.wait_ge(qks_in.sem, qks_in.at(l))
                dve.wait_ge(rot.sem, rot.at(l * TILES - 1))
                for i in range(4):
                    nc.vector.tensor_tensor(rope[:, i], rope0[:, i],
                                            qks[:, i:i + 1, :].to_broadcast([P, TPB, DH]), ALU.mult)\
                        .then_inc(rope_t.sem, 1)
                dve.wait_ge(rope_t.sem, rope_t.at(l))
                rotate(l * TILES, 0, 0, 1)
                with dve.Fori(0, TPB - 1) as p:
                    for u in range(2):
                        n = l * TILES + p * 2 + u
                        soften(n, u)
                        rotate(n + 1, p if u == 0 else p + 1, 1 - u, u)
                        finish(n, p, u)
                n = l * TILES + TILES - 2
                soften(n, 0)
                rotate(n + 1, TPB - 1, 1, 0)
                finish(n, TPB - 1, 0)
                soften(n + 1, 1)
                finish(n + 1, TPB - 1, 1)
                dve.wait_ge(ffn_in.sem, ffn_in.at(l))
                for b in range(NBLK):
                    feed(l, b)
            dve.wait_ge(h_new.sem, h_new.at((first + DEPTH) * NBLK - 1))
            for b in range(B):
                nc.vector.tensor_tensor(X[:, b * T:(b + 1) * T], X[:, b * T:(b + 1) * T],
                                        H[:, b * SEQ + 1:(b + 1) * SEQ], ALU.add).then_inc(x_add.sem, 1)


def tile_of(p, u):
    return (p & (TPB // 2 - 1)) * 2 + u


def tile_col(p, u):
    return p * (2 * P) + u * P + ((p >> 2) & 1)


def constants():
    f = np.float32
    half = np.arange(0, DH, 2, dtype=f)
    inv_freq = (f(1.0) / np.power(f(10000.0), half / f(DH))).astype(f)
    t = np.arange(T, dtype=f)
    fr = t[:, None] * inv_freq[None, :]
    base = ((half + f(0.4 * DH)) / f(1.4 * DH)).astype(f)
    power = (t - f(T // 2)) / f(W // 2)
    scale = np.power(base[None, :], power[:, None]).astype(f)
    cos, sin = np.cos(fr).astype(f), np.sin(fr).astype(f)
    fq, fk = scale * f(8.0), f(1.0) / scale
    tabs = []
    for s in (fq, fk):
        tabs.append(np.concatenate([cos * s, cos * s], 1))
        tabs.append(np.concatenate([-sin * s, sin * s], 1))
    rope = np.stack(tabs).reshape(4, TPB, P, DH).transpose(2, 0, 1, 3)

    def bf(a):
        return (np.ascontiguousarray(a, f).view(np.uint32) >> 16).astype(np.uint16)

    band = np.zeros((P, TPB, 2 * W), f)
    a = (np.arange(P) % W)[:, None]
    j = np.arange(2 * W)[None, :]
    band[:, :, :] = np.where((j < a) | (j > a + W), f(NEG), f(0))[:, None, :]
    band[0:W, 0, 0:W] = NEG
    keep = np.ones((P, TPB), f)
    keep[:, TPB - 1] = 0
    i, j = np.arange(P)[:, None], np.arange(P)[None, :]
    return {
        "ident": np.eye(P, dtype=f), "ident16": bf(np.eye(P)), "rope": np.ascontiguousarray(rope),
        "band": bf(band), "keep": keep,
        "Amask": bf(np.where(i > j, f(NEG), f(0))),
        "Bmask": bf(np.where(j > i, f(NEG), f(0))),
    }


def kernel(**inputs):
    import concourse.bacc as _bacc
    from concourse.bass_utils import run_bass_kernel_spmd as _run

    a = {k: np.ascontiguousarray(np.asarray(v)) for k, v in inputs.items()}
    wa = a["L0_attn_a_W_attn"]
    data = {"L0_attn_a_x": a["L0_attn_a_x"], "Awo": a["L0_attn_a_W_proj"]}
    for i, x in enumerate("qkv"):
        data[f"Aw{x}"] = np.ascontiguousarray(wa[:, i * C:(i + 1) * C])
    for x, name in (("q", "q_heads"), ("k", "k_heads"), ("v", "v_heads"), ("o", "output_proj")):
        data[f"Bw{x}"] = np.ascontiguousarray(a[f"L0_attn_b_{name}"].T)
    for k in FFN_PARAMS:
        data[k] = a[k]
    data.update(constants())

    nc = _bacc.Bacc("TRN2", target_bir_lowering=False, num_devices=1)
    ins, arrays = {}, {}
    for k, v in data.items():
        arrays[f"in_{k}"] = v
        ins[k] = nc.dram_tensor(f"in_{k}", v.shape, mybir.dt.from_np(v.dtype), kind="ExternalInput").ap()
    outs = {"out": nc.dram_tensor("out_x", (B, T, C), FP32, kind="ExternalOutput").ap()}
    build_stack_kernel(nc, ins, outs)
    r = _run(nc, [arrays], core_ids=[0])
    return r.results[0]["out_x"]
```
